# Optimizing a Trainium2 kernel written in Bass

```python
import numpy as np
import jax
import jax.numpy as jnp

def _softmax(x, axis=-1):
    return jax.nn.softmax(x, axis=axis)
def _gelu(x):
    return jax.nn.gelu(x, approximate=True)
def _silu(x):
    return jax.nn.silu(x)
def _sigmoid(x):
    return jax.nn.sigmoid(x)
def _layernorm(x, axis=-1, eps=1e-5):
    m = jnp.mean(x, axis=axis, keepdims=True)
    v = jnp.var(x, axis=axis, keepdims=True)
    return (x - m) / jnp.sqrt(v + eps)
def _scatter_add(tgt, idx, src, axis=0):
    return tgt.at[idx].add(src)
def _segment_sum(src, seg, n):
    return jax.ops.segment_sum(src, seg, n)

kernel_name = 'mk_adj_preln_d1_adj_64_7ad53e'

def setup_inputs(seed: int = 0):
    np.random.seed(seed)
    _w = jnp.asarray
    def _rec_inputs():
        import jax
        import jax.numpy as jnp
        _gk = jax.random.key(seed)
        x = -9.806e-05 + 1 * jax.random.normal(jax.random.fold_in(_gk, 1), (8192, 64), jnp.float32)
        _a = jax.random.bernoulli(jax.random.fold_in(_gk, 2), 0.000488281, (8192, 8192))
        _a = jnp.logical_or(_a, jnp.swapaxes(_a, -1, -2))
        _a = jnp.logical_or(_a, jnp.eye(8192, dtype=bool))
        adj = _a.astype(jnp.int32)
        return x, adj
    x, adj = _rec_inputs()
    def _L0_gnn_setup():
        import jax, jax.numpy as jnp
        import numpy as np
        ALPHA = 0.2
        NEG_BIG = -9000000000000000.0
        key = jax.random.key(seed)
        k1, k2, k3, k4, k5 = jax.random.split(key, 5)
        N, M, F_in, F_out = (8192, 8192, 64, 64)
        item_embs = jax.random.normal(k1, (N, F_in), dtype=jnp.float32)
        entity_embs = jax.random.normal(k2, (M, F_in), dtype=jnp.float32)
        adj = jax.random.randint(k3, (N, M), 0, 2, dtype=jnp.int32)
        W = jax.random.normal(k4, (F_in, F_out), dtype=jnp.float32)
        a = jax.random.normal(k5, (2 * F_out, 1), dtype=jnp.float32)
        return {'item_embs': item_embs, 'entity_embs': entity_embs, 'adj': adj, 'W': W, 'a': a}
    _L0_gnn_all = _L0_gnn_setup()
    _L0_gnn_in = {k: v for k, v in _L0_gnn_all.items() if k in ('entity_embs', 'W', 'a', )}
    del _L0_gnn_all

    return {
        "x": x,
        "adj": adj,
        "L0_gnn_entity_embs": _L0_gnn_in["entity_embs"],
        "L0_gnn_W": _L0_gnn_in["W"],
        "L0_gnn_a": _L0_gnn_in["a"],
    }

def reference(x, adj, L0_gnn_entity_embs, L0_gnn_W, L0_gnn_a):
    import jax
    import jax.numpy as jnp
    def _L0_gnn_ref(item_embs, entity_embs, adj, W, a):
        import jax, jax.numpy as jnp
        import numpy as np
        ALPHA = 0.2
        NEG_BIG = -9000000000000000.0
        F_out = W.shape[1]
        Wh = item_embs @ W
        We = entity_embs @ W
        a1 = a[:F_out, 0]
        a2 = a[F_out:, 0]
        scores = (Wh @ a1)[:, None] + (We @ a2)[None, :]
        e = jnp.where(scores > 0, scores, ALPHA * scores)
        e = jnp.where(adj > 0, e, NEG_BIG)
        attention = jax.nn.softmax(e, axis=1)
        entity_emb_weighted = attention @ entity_embs
        h_prime = entity_emb_weighted + item_embs
        return jax.nn.elu(h_prime)

    h = jnp.maximum(_layernorm(x, axis=-1), 0.0)
    x = x + _L0_gnn_ref(h, L0_gnn_entity_embs, adj, L0_gnn_W, L0_gnn_a)
    return x


_drawn_inputs = setup_inputs


def setup_inputs(seed=0):
    import zlib

    import numpy as np

    out = dict(_drawn_inputs(seed))
    spreads = {}
    factors = {}
    for name, (base, spread) in spreads.items():
        noise = np.random.default_rng([zlib.crc32(name.encode()), seed]).standard_normal(out[name].shape)
        drawn = base * np.exp(spread * noise) if base else spread * noise
        out[name] = jnp.asarray(drawn.astype(out[name].dtype))
    for name, factor in factors.items():
        out[name] = (out[name] * factor).astype(out[name].dtype)
    return out
```

```python
import concourse.bass as bass
from concourse import mybir
from contextlib import ExitStack


def graph_attention_kernel(nc, x, adj, entity, W, a, out):
    F32, BF16, I32 = mybir.dt.float32, mybir.dt.bfloat16, mybir.dt.int32
    ALU = mybir.AluOpType
    ACT = mybir.ActivationFunctionType
    AX = mybir.AxisListType

    P = nc.NUM_PARTITIONS
    N, F = x.shape
    M = entity.shape[0]
    NT = N // P
    NJ = M // P
    CH = 2048
    NC = M // CH
    BLK = 1024
    NB = M // BLK
    JB = BLK // P
    BPC = CH // BLK
    FA = F + 1
    BANK = 512
    SLOPE = 0.2
    UNIT = 2.0 ** -60
    EPS = 1e-5
    LOWEST = -3.0e38
    RING = 3
    ROUNDS = NT // RING
    PEELED = 2

    with ExitStack() as es:
        def sb(name, shape, dt=F32):
            return es.enter_context(nc.sbuf_tensor(name, shape, dt))

        def ps(name, shape):
            return es.enter_context(nc.psum_tensor(name, shape, F32))

        def sem(name):
            return es.enter_context(nc.semaphore(name))

        logits = sb("logits", [P, RING, M])
        adj_buf = sb("adj_buf", [P, 2, CH], I32)
        mask_buf = sb("mask_buf", [P, 2, CH], BF16)
        relu_buf = sb("relu_buf", [P, 2, CH])
        s2_rows = sb("s2_rows", [P, M])
        ent = sb("ent", [P, NJ, FA])
        weights = sb("weights", [P, 2, JB, P])
        ident = sb("ident", [P, P])
        w_sb = sb("w_sb", [F, F])
        wT_sb = sb("wT_sb", [F, F])
        a_sb = sb("a_sb", [F, 2])
        a_wide = sb("a_wide", [F, 2, P])
        u2_wide = sb("u2_wide", [F, P])
        u1_rows = sb("u1_rows", [P, 1, F])
        mean = sb("mean", [P, NT])
        var = sb("var", [P, NT])
        stats = sb("stats", [P, NT, 3])
        row = sb("row", [P, RING, 3])
        chunk_max = sb("chunk_max", [P, RING, NC])
        row_max = sb("row_max", [P, RING])
        row_lin = sb("row_lin", [P, RING])
        row_w = sb("row_w", [P, RING])
        sumsT_sb = sb("sumsT_sb", [FA, P])
        inv_den = sb("inv_den", [P, 1])
        x_tile = sb("x_tile", [P, RING, F])
        h_tile = sb("h_tile", [P, RING, F])
        y_tile = sb("y_tile", [P, RING, F])
        neg_tile = sb("neg_tile", [P, RING, F])
        exp_tile = sb("exp_tile", [P, RING, F])
        ones_tile = sb("ones_tile", [P, F])
        out_tile = sb("out_tile", [P, RING, F])

        turned = ps("turned", [P, 2, JB, P])
        sumsT = ps("sumsT", [P, RING, BANK])
        sums = ps("sums", [P, BANK])

        x_all = logits[:, 2, 0:NT * F].rearrange("p (t f) -> p t f", f=F)
        tmp_all = logits[:, 2, NT * F:2 * NT * F].rearrange("p (t f) -> p t f", f=F)
        entT = logits[0:F, 1, :]
        s1x08, rstd, shift = stats[:, :, 0], stats[:, :, 1], stats[:, :, 2]
        wT_ps, u2_ps, u1_ps = sums[0:F, 0:F], sums[0:F, P:2 * P], sums[:, 2 * P:2 * P + F]

        params_here, ent_here, x_all_here = sem("params_here"), sem("ent_here"), sem("x_all_here")
        adj_here = [sem("adj_here0"), sem("adj_here1")]
        x_here = [sem(f"x_here{k}") for k in range(RING)]
        stored = [sem(f"stored{k}") for k in range(RING)]
        ident_step, ones_ready = sem("ident_step"), sem("ones_ready")
        wT_turned, wT_copied, wide_ready = sem("wT_turned"), sem("wT_copied"), sem("wide_ready")
        u_done, u_copied = sem("u_done"), sem("u_copied")
        entT_turned, entT_copied = sem("entT_turned"), sem("entT_copied")
        s2_done, s2_copied = sem("s2_done"), sem("s2_copied")
        ln_step, std_ready = sem("ln_step"), sem("std_ready")
        mask_ready, z_ready, relu_ready = sem("mask_ready"), sem("z_ready"), sem("relu_ready")
        row_step, shifted = sem("row_step"), sem("shifted")
        block_turned, weights_ready = sem("block_turned"), sem("weights_ready")
        block_summed, sumsT_copied = sem("block_summed"), sem("sumsT_copied")
        sums_turned, den_ready = sem("sums_turned"), sem("den_ready")
        h_ready, y_ready, neg_ready = sem("h_ready"), sem("y_ready"), sem("neg_ready")
        exp_ready, out_step = sem("exp_ready"), sem("out_step")

        block = es.enter_context(nc.Block())

        LN_STEPS = 11
        NS = M // BANK
        ROW_STEPS = 4
        OUT_STEPS = 4
        STORE_LAG = 5

        def periods(engine, body, last):
            for t in range(PEELED * RING):
                body(t, t % RING, t // RING)
            with engine.Fori(PEELED, ROUNDS, 1) as r:
                for k in range(RING):
                    body(r * RING + k, k, r)
            for t in range(ROUNDS * RING, last):
                body(t, t % RING, t // RING)

        def known_below(t, bound):
            return isinstance(t, int) and t < bound

        def in_range(t):
            return not isinstance(t, int) or 0 <= t < NT

        @block.sync
        def _(sp):
            sp.dma_start(w_sb[:, :], W[:, :]).then_inc(params_here, 16)
            for k in range(2):
                sp.dma_start(a_sb[:, k:k + 1], a[k * F:(k + 1) * F, :]).then_inc(params_here, 16)
            sp.dma_start(ent[:, :, 0:F], entity.rearrange("(c p) f -> p c f", p=P)).then_inc(ent_here, 16)
            sp.dma_start(x_all, x.rearrange("(t p) f -> p t f", p=P)).then_inc(x_all_here, 16)

            def load_tile(t):
                for c in range(NC):
                    if not known_below(t, 1) or c >= 2:
                        sp.wait_ge(mask_ready, NC * t + c - 1)
                    sp.dma_start(adj_buf[:, c % 2, :],
                                 adj[bass.ds(t * P, P), c * CH:(c + 1) * CH]).then_inc(adj_here[c % 2], 16)

            def load_x(t, slot):
                if not known_below(t, RING):
                    sp.wait_ge(out_step, OUT_STEPS * (t - RING + 1))
                sp.dma_start(x_tile[:, slot, :], x[bass.ds(t * P, P), :]).then_inc(x_here[slot], 16)

            def store_out(t, slot):
                sp.wait_ge(out_step, OUT_STEPS * (t + 1))
                sp.dma_start(out[bass.ds(t * P, P), :], out_tile[:, slot, :]).then_inc(stored[slot], 16)

            def period(t, slot, r):
                if in_range(t - STORE_LAG):
                    store_out(t - STORE_LAG, (slot - STORE_LAG) % RING)
                if in_range(t - 1):
                    load_x(t - 1, (slot - 1) % RING)
                if in_range(t):
                    load_tile(t)

            periods(sp, period, NT + STORE_LAG)
            for slot in range(RING):
                sp.wait_ge(stored[slot], 16 * len(range(slot, NT, RING)))

        @block.gpsimd
        def _(pool):
            pool.memset(ent[:, :, F:FA], 1.0).then_inc(ones_ready, 1)
            pool.memset(ident[:, :], 0.0).then_inc(ident_step, 1)
            pool.wait_ge(ident_step, 1)
            pool.affine_select(out=ident[:, :], in_=ident[:, :], compare_op=ALU.not_equal, fill=1.0,
                               base=0, pattern=[[-1, P]], channel_multiplier=1).then_inc(ident_step, 1)
            pool.memset(ones_tile[:, :], 1.0).then_inc(ones_ready, 1)
            pool.wait_ge(ones_ready, 2)

            def finish(t, slot, r):
                if not known_below(t, RING):
                    pool.wait_ge(stored[slot], 16 * r)
                pool.wait_ge(neg_ready, t + 1)
                pool.tensor_tensor(out_tile[:, slot, :], y_tile[:, slot, :], neg_tile[:, slot, :],
                                   ALU.add).then_inc(out_step, 1)
                pool.wait_ge(exp_ready, t + 1)
                pool.tensor_tensor(exp_tile[:, slot, :], exp_tile[:, slot, :], ones_tile[:, :],
                                   ALU.subtract).then_inc(out_step, 1)
                pool.wait_ge(out_step, OUT_STEPS * t + 2)
                pool.tensor_tensor(out_tile[:, slot, :], out_tile[:, slot, :], exp_tile[:, slot, :],
                                   ALU.add).then_inc(out_step, 1)
                pool.wait_ge(out_step, OUT_STEPS * t + 3)
                pool.tensor_tensor(out_tile[:, slot, :], out_tile[:, slot, :], x_tile[:, slot, :],
                                   ALU.add).then_inc(out_step, 1)

            periods(pool, finish, NT)

        @block.scalar
        def _(act):
            for q in range(NS):
                act.wait_ge(entT_turned, q + 1)
                nc.scalar.activation(entT[:, q * BANK:(q + 1) * BANK],
                                     turned[0:F, q % 2, 0:BANK // P, :], ACT.Copy).then_inc(entT_copied, 1)
            act.wait_ge(ln_step, 6)
            nc.scalar.activation(rstd, var[:, :], ACT.Sqrt).then_inc(std_ready, 1)

            def make_relu(t, slot, c):
                n = NC * t + c
                act.wait_ge(z_ready, n + 1)
                if not known_below(t, 1) or c >= 2:
                    act.wait_ge(shifted, n - 1)
                act.wait_ge(row_step, ROW_STEPS * t + 1)
                nc.scalar.activation(relu_buf[:, c % 2, :], logits[:, slot, c * CH:(c + 1) * CH], ACT.Relu,
                                     bias=row[:, slot, 0:1], scale=4.0).then_inc(relu_ready, 1)

            def make_weights(t, c):
                for b in range(c * BPC, (c + 1) * BPC):
                    act.wait_ge(block_turned, NB * t + b + 1)
                    if not known_below(t, 1) or b >= 2:
                        act.wait_ge(block_summed, NB * t + b - 1)
                    nc.scalar.activation(weights[:, b % 2, :, :], turned[:, b % 2, :, :],
                                         ACT.Exp).then_inc(weights_ready, 1)

            def make_h(t, slot, r):
                act.wait_ge(x_here[slot], 16 * (r + 1))
                if not known_below(t, RING):
                    act.wait_ge(y_ready, t - RING + 1)
                act.wait_ge(row_step, ROW_STEPS * t + 1)
                nc.scalar.activation(h_tile[:, slot, :], x_tile[:, slot, :], ACT.Relu,
                                     bias=row[:, slot, 2:3], scale=row[:, slot, 1:2]).then_inc(h_ready, 1)

            def make_exp(t, slot):
                act.wait_ge(y_ready, t + 1)
                if not known_below(t, RING):
                    act.wait_ge(out_step, OUT_STEPS * (t - RING + 1))
                nc.scalar.activation(neg_tile[:, slot, :], y_tile[:, slot, :], ACT.Relu,
                                     scale=-1.0).then_inc(neg_ready, 1)
                act.wait_ge(neg_ready, t + 1)
                nc.scalar.activation(exp_tile[:, slot, :], neg_tile[:, slot, :], ACT.Exp,
                                     scale=-1.0).then_inc(exp_ready, 1)

            def period(t, slot, r):
                for c in range(NC):
                    if in_range(t - 1):
                        make_relu(t - 1, (slot - 1) % RING, c)
                    if c == 0 and in_range(t - 2):
                        make_weights(t - 2, NC - 1)
                    if c > 0 and in_range(t - 1):
                        make_weights(t - 1, c - 1)
                    if c == 2 and in_range(t - 3):
                        make_exp(t - 3, slot)
                    if c == 3 and in_range(t - 1):
                        make_h(t - 1, (slot - 1) % RING, r if slot else r - 1)

            periods(act, period, NT + 3)

        @block.vector
        def _(dve):
            dve.wait_ge(params_here, 48)
            for k in range(2):
                dve.tensor_copy(a_wide[:, k, :], a_sb[:, k:k + 1].to_broadcast([F, P])).then_inc(wide_ready, 1)
            dve.wait_ge(wT_turned, 1)
            dve.tensor_copy(wT_sb[:, :], wT_ps).then_inc(wT_copied, 1)
            dve.wait_ge(u_done, 2)
            dve.tensor_copy(u2_wide[:, :], u2_ps).then_inc(u_copied, 1)
            dve.tensor_copy(u1_rows[:, 0, :], u1_ps).then_inc(u_copied, 1)

            def wide(col):
                return col.rearrange("p (t o) -> p t o", o=1).to_broadcast([P, NT, F])

            dve.wait_ge(x_all_here, 16)
            dve.tensor_reduce(mean[:, :], x_all, AX.X, ALU.add).then_inc(ln_step, 1)
            dve.wait_ge(ln_step, 1)
            dve.tensor_scalar(mean[:, :], mean[:, :], 1.0 / F, None, ALU.mult).then_inc(ln_step, 1)
            dve.wait_ge(ln_step, 2)
            dve.tensor_tensor(x_all, x_all, wide(mean[:, :]), ALU.subtract).then_inc(ln_step, 1)
            dve.wait_ge(ln_step, 3)
            dve.tensor_tensor(tmp_all, x_all, x_all, ALU.mult).then_inc(ln_step, 1)
            dve.wait_ge(ln_step, 4)
            dve.tensor_reduce(var[:, :], tmp_all, AX.X, ALU.add).then_inc(ln_step, 1)
            dve.wait_ge(ln_step, 5)
            dve.tensor_scalar(var[:, :], var[:, :], 1.0 / F, EPS, ALU.mult, ALU.add).then_inc(ln_step, 1)
            for q in range(NS):
                dve.wait_ge(s2_done, q + 1)
                dve.tensor_scalar(s2_rows[:, q * BANK:(q + 1) * BANK], sumsT[:, q % RING, :], UNIT, None,
                                  ALU.mult).then_inc(s2_copied, 1)
            dve.wait_ge(std_ready, 1)
            dve.reciprocal(rstd, rstd).then_inc(ln_step, 1)
            dve.wait_ge(ln_step, 7)
            dve.scalar_tensor_tensor(out=shift, in0=mean[:, :], scalar=-1.0, in1=rstd,
                                     op0=ALU.mult, op1=ALU.mult)
            dve.tensor_tensor(tmp_all, x_all, wide(rstd), ALU.mult).then_inc(ln_step, 1)
            dve.wait_ge(ln_step, 8)
            dve.wait_ge(u_copied, 2)
            dve.scalar_tensor_tensor(out=tmp_all, in0=tmp_all, scalar=0.0,
                                     in1=u1_rows[:, :, :].to_broadcast([P, NT, F]),
                                     op0=ALU.max, op1=ALU.mult).then_inc(ln_step, 1)
            dve.wait_ge(ln_step, 9)
            dve.tensor_reduce(s1x08, tmp_all, AX.X, ALU.add).then_inc(ln_step, 1)
            dve.wait_ge(ln_step, 10)
            dve.tensor_scalar(s1x08, s1x08, 1.0 - SLOPE, None, ALU.mult).then_inc(ln_step, 1)
            dve.wait_ge(ln_step, 11)

            def make_mask(t, c):
                n = NC * t + c
                dve.wait_ge(adj_here[c % 2], 16 * (NC // 2 * t + c // 2 + 1))
                if not known_below(t, 1) or c >= 2:
                    dve.wait_ge(z_ready, n - 1)
                dve.tensor_scalar(mask_buf[:, c % 2, :], adj_buf[:, c % 2, :], 0.0, None,
                                  ALU.is_le).then_inc(mask_ready, 1)

            def make_z(t, slot, c):
                dve.wait_ge(mask_ready, NC * t + c + 1)
                if not known_below(t, RING):
                    dve.wait_ge(block_turned, NB * (t - RING) + BPC * (c + 1))
                if c + 1 < NC:
                    make_mask(t, c + 1)
                elif in_range(t + 1):
                    make_mask(t + 1, 0)
                cols = slice(c * CH, (c + 1) * CH)
                dve.tensor_tensor_reduce(out=logits[:, slot, cols], in0=s2_rows[:, cols],
                                         in1=mask_buf[:, c % 2, :], scale=SLOPE / UNIT, scalar=LOWEST,
                                         op0=ALU.subtract, op1=ALU.max,
                                         accum_out=chunk_max[:, slot, c:c + 1]).then_inc(z_ready, 1)

            def make_shift(t, slot):
                if not known_below(t, RING):
                    dve.wait_ge(h_ready, t - RING + 1)
                dve.tensor_copy(row[:, slot, :], stats[:, bass.ds(t, 1), :].squeeze(1)).then_inc(row_step, 1)
                dve.wait_ge(z_ready, NC * (t + 1))
                dve.tensor_reduce(row_max[:, slot:slot + 1], chunk_max[:, slot, :], AX.X,
                                  ALU.max).then_inc(row_step, 1)
                dve.wait_ge(row_step, ROW_STEPS * t + 2)
                dve.tensor_scalar(row_lin[:, slot:slot + 1], row_max[:, slot:slot + 1], 4.0,
                                  row[:, slot, 0:1], ALU.mult, ALU.add).then_inc(row_step, 1)
                dve.wait_ge(row_step, ROW_STEPS * t + 3)
                dve.scalar_tensor_tensor(out=row_w[:, slot:slot + 1], in0=row_lin[:, slot:slot + 1], scalar=0.0,
                                         in1=row_max[:, slot:slot + 1], op0=ALU.max,
                                         op1=ALU.add).then_inc(row_step, 1)

            def shift_logits(t, slot, c):
                dve.wait_ge(row_step, ROW_STEPS * (t + 1))
                dve.wait_ge(relu_ready, NC * t + c + 1)
                cols = slice(c * CH, (c + 1) * CH)
                dve.scalar_tensor_tensor(out=logits[:, slot, cols], in0=logits[:, slot, cols],
                                         scalar=row_w[:, slot:slot + 1], in1=relu_buf[:, c % 2, :],
                                         op0=ALU.subtract, op1=ALU.add).then_inc(shifted, 1)

            def copy_sums(t, slot):
                dve.wait_ge(block_summed, NB * (t + 1))
                if not known_below(t, 1):
                    dve.wait_ge(sums_turned, t)
                dve.tensor_copy(sumsT_sb[:, :], sumsT[0:FA, slot, 0:P]).then_inc(sumsT_copied, 1)

            def make_y(t, slot):
                dve.wait_ge(sums_turned, t + 1)
                dve.reciprocal(inv_den[:, :], sums[:, F:FA]).then_inc(den_ready, 1)
                dve.wait_ge(den_ready, t + 1)
                dve.wait_ge(h_ready, t + 1)
                if not known_below(t, RING):
                    dve.wait_ge(out_step, OUT_STEPS * (t - RING + 1))
                dve.scalar_tensor_tensor(out=y_tile[:, slot, :], in0=sums[:, 0:F], scalar=inv_den[:, :],
                                         in1=h_tile[:, slot, :], op0=ALU.mult, op1=ALU.add).then_inc(y_ready, 1)

            def period(t, slot, r):
                for c in range(NC):
                    if in_range(t):
                        make_z(t, slot, c)
                    if in_range(t - 1):
                        shift_logits(t - 1, (slot - 1) % RING, c)
                    if c == 1 and in_range(t - 2):
                        copy_sums(t - 2, (slot - 2) % RING)
                    if c == 3 and in_range(t - 2):
                        make_y(t - 2, (slot - 2) % RING)
                if in_range(t):
                    make_shift(t, slot)

            make_mask(0, 0)
            periods(dve, period, NT + 2)

        @block.tensor
        def _(pe):
            pe.wait_ge(params_here, 48)
            pe.wait_ge(ident_step, 2)
            pe.transpose(wT_ps, w_sb[:, :], ident[0:F, 0:F]).then_inc(wT_turned, 1)
            pe.wait_ge(ent_here, 16)
            pe.wait_ge(wide_ready, 2)
            pe.wait_ge(wT_copied, 1)
            pe.matmul(u2_ps, wT_sb[:, :], a_wide[:, 1, :], start=True, stop=True).then_inc(u_done, 1)
            pe.matmul(u1_ps, a_wide[:, 0, :], wT_sb[:, :], start=True, stop=True).then_inc(u_done, 1)

            def turn_entities(q):
                if q >= 2:
                    pe.wait_ge(entT_copied, q - 1)
                for k in range(BANK // P):
                    last = pe.transpose(turned[0:F, q % 2, k, :], ent[:, q * (BANK // P) + k, 0:F], ident[:, :])
                last.then_inc(entT_turned, 1)

            turn_entities(0)
            pe.wait_ge(u_copied, 1)
            for q in range(NS):
                if q + 1 < NS:
                    turn_entities(q + 1)
                pe.wait_ge(entT_copied, q + 1)
                if q >= RING:
                    pe.wait_ge(s2_copied, q - RING + 1)
                pe.matmul(sumsT[:, q % RING, :], u2_wide[:, :], entT[:, q * BANK:(q + 1) * BANK],
                          start=True, stop=True).then_inc(s2_done, 1)
            pe.wait_ge(s2_copied, NS)
            pe.wait_ge(ones_ready, 1)

            def turn_block(t, slot, b):
                pe.wait_ge(shifted, NC * t + b // BPC + 1)
                if not known_below(t, 1) or b >= 2:
                    pe.wait_ge(weights_ready, NB * t + b - 1)
                for k in range(JB):
                    j = b * BLK + k * P
                    last = pe.transpose(turned[:, b % 2, k, :], logits[:, slot, j:j + P], ident[:, :])
                last.then_inc(block_turned, 1)

            def sum_block(t, slot, b):
                pe.wait_ge(weights_ready, NB * t + b + 1)
                if b == 0 and not known_below(t, RING):
                    pe.wait_ge(sumsT_copied, t - RING + 1)
                for k in range(JB):
                    g = b * JB + k
                    last = pe.matmul(sumsT[0:FA, slot, 0:P], ent[:, g, :], weights[:, b % 2, k, :],
                                     start=(g == 0), stop=(g == NJ - 1))
                last.then_inc(block_summed, 1)

            def turn_back(t):
                pe.wait_ge(sumsT_copied, t + 1)
                if not known_below(t, 1):
                    pe.wait_ge(y_ready, t)
                pe.transpose(sums[:, 0:FA], sumsT_sb[:, :], ident[0:FA, 0:FA]).then_inc(sums_turned, 1)

            def period(t, slot, r):
                if in_range(t):
                    turn_block(t, slot, 0)
                for b in range(NB):
                    if in_range(t):
                        if b + 1 < NB:
                            turn_block(t, slot, b + 1)
                        sum_block(t, slot, b)
                    if b == 4 and in_range(t - 1):
                        turn_back(t - 1)

            periods(pe, period, NT + 1)


_INS = ['x', 'adj', 'L0_gnn_entity_embs', 'L0_gnn_W', 'L0_gnn_a']


def kernel(**inputs):
    import numpy as _np
    import concourse.bacc as _bacc
    from concourse import mybir as _mybir
    from concourse.bass_utils import run_bass_kernel_spmd as _run

    nc = _bacc.Bacc("TRN2", target_bir_lowering=False, num_devices=1)
    arrays, args = {}, []
    for name in _INS:
        v = _np.ascontiguousarray(inputs[name])
        arrays[f"in_{name}"] = v
        args.append(nc.dram_tensor(f"in_{name}", v.shape, _mybir.dt.from_np(v.dtype), kind="ExternalInput").ap())
    args.append(nc.dram_tensor("out_0", inputs['x'].shape, _mybir.dt.float32, kind="ExternalOutput").ap())
    graph_attention_kernel(nc, *args)
    r = _run(nc, [arrays], core_ids=[0])
    return r.results[0]["out_0"]
```

```python
import concourse.bass as bass
from concourse import mybir
from contextlib import ExitStack


def graph_attention_kernel(nc, x, adj, entity, W, a, out):
    F32, BF16, I32 = mybir.dt.float32, mybir.dt.bfloat16, mybir.dt.int32
    ALU = mybir.AluOpType
    ACT = mybir.ActivationFunctionType
    AX = mybir.AxisListType

    P = nc.NUM_PARTITIONS
    N, F = x.shape
    M = entity.shape[0]
    NT = N // P
    NJ = M // P
    CH = 2048
    NC = M // CH
    BLK = 1024
    NB = M // BLK
    JB = BLK // P
    BPC = CH // BLK
    FA = F + 1
    BANK = 512
    SLOPE = 0.2
    UNIT = 2.0 ** -60
    EPS = 1e-5
    LOWEST = -3.0e38
    HUGE = 2.0 ** 40
    RING = 3
    ROUNDS = NT // RING
    PEELED = 3

    with ExitStack() as es:
        def sb(name, shape, dt=F32):
            return es.enter_context(nc.sbuf_tensor(name, shape, dt))

        def ps(name, shape):
            return es.enter_context(nc.psum_tensor(name, shape, F32))

        def sem(name):
            return es.enter_context(nc.semaphore(name))

        logits = sb("logits", [P, RING, M])
        adj_buf = sb("adj_buf", [P, 2, CH], I32)
        mask_buf = sb("mask_buf", [P, 2, CH], BF16)
        relu_buf = sb("relu_buf", [P, 2, CH])
        s2_rows = sb("s2_rows", [P, M])
        ent = sb("ent", [P, NJ, FA])
        weights = sb("weights", [P, 2, JB, P])
        ident = sb("ident", [P, P])
        w_sb = sb("w_sb", [F, F])
        wT_sb = sb("wT_sb", [F, F])
        a_sb = sb("a_sb", [F, 2])
        a_wide = sb("a_wide", [F, 2, P])
        u2_wide = sb("u2_wide", [F, P])
        u1_rows = sb("u1_rows", [P, 1, F])
        mean = sb("mean", [P, NT])
        var = sb("var", [P, NT])
        stats = sb("stats", [P, NT, 3])
        row = sb("row", [P, RING, 3])
        chunk_max = sb("chunk_max", [P, RING, NC])
        row_max = sb("row_max", [P, RING])
        row_lin = sb("row_lin", [P, RING])
        row_w = sb("row_w", [P, RING])
        row_bare = sb("row_bare", [P, RING])
        sumsT_sb = sb("sumsT_sb", [FA, P])
        inv_den = sb("inv_den", [P, 1])
        full_sums = sb("full_sums", [P, FA])
        ent_sum = sb("ent_sum", [P, FA])
        ones = sb("ones", [P, P])
        x_tile = sb("x_tile", [P, RING, F])
        h_tile = sb("h_tile", [P, RING, F])
        y_tile = sb("y_tile", [P, RING, F])
        neg_tile = sb("neg_tile", [P, RING, F])
        exp_tile = sb("exp_tile", [P, RING, F])
        out_tile = sb("out_tile", [P, RING, F])

        turned = ps("turned", [P, 2, JB, P])
        sumsT = ps("sumsT", [P, RING, BANK])
        sums = ps("sums", [P, BANK])

        x_all = logits[:, 2, 0:NT * F].rearrange("p (t f) -> p t f", f=F)
        tmp_all = logits[:, 2, NT * F:2 * NT * F].rearrange("p (t f) -> p t f", f=F)
        entT = logits[0:F, 1, :]
        s1x08, rstd, shift = stats[:, :, 0], stats[:, :, 1], stats[:, :, 2]
        wT_ps, u2_ps, u1_ps = sums[0:F, 0:F], sums[0:F, P:2 * P], sums[:, 2 * P:2 * P + F]
        ent_sum_ps = sums[:, 3 * P:3 * P + FA]

        params_here, ent_here, x_all_here = sem("params_here"), sem("ent_here"), sem("x_all_here")
        adj_here = [sem("adj_here0"), sem("adj_here1")]
        x_here = [sem(f"x_here{k}") for k in range(RING)]
        stored = [sem(f"stored{k}") for k in range(RING)]
        ident_step, ones_ready = sem("ident_step"), sem("ones_ready")
        wT_turned, wT_copied, wide_ready = sem("wT_turned"), sem("wT_copied"), sem("wide_ready")
        u_done, u_copied = sem("u_done"), sem("u_copied")
        entT_turned, entT_copied = sem("entT_turned"), sem("entT_copied")
        s2_done, s2_copied = sem("s2_done"), sem("s2_copied")
        ln_step, std_ready = sem("ln_step"), sem("std_ready")
        mask_ready = [sem("mask_ready0"), sem("mask_ready1")]
        z_ready, relu_ready = sem("z_ready"), sem("relu_ready")
        row_copied, row_step, shifted = sem("row_copied"), sem("row_step"), sem("shifted")
        block_turned, weights_ready = sem("block_turned"), sem("weights_ready")
        block_summed, sumsT_copied = sem("block_summed"), sem("sumsT_copied")
        sums_turned, y_step = sem("sums_turned"), sem("y_step")
        ent_summed, ent_sum_copied = sem("ent_summed"), sem("ent_sum_copied")
        h_ready, y_ready, neg_ready = sem("h_ready"), sem("y_ready"), sem("neg_ready")
        exp_ready, out_step = sem("exp_ready"), sem("out_step")

        block = es.enter_context(nc.Block())

        LN_STEPS = 11
        NS = M // BANK
        ROW_STEPS = 4
        OUT_STEPS = 4
        Y_STEPS = 2

        def periods(engine, body, last):
            for t in range(PEELED * RING):
                body(t, t % RING, t // RING)
            with engine.Fori(PEELED, ROUNDS, 1) as r:
                for k in range(RING):
                    body(r * RING + k, k, r)
            for t in range(ROUNDS * RING, last):
                body(t, t % RING, t // RING)

        def mask_by_vector(slot, c):
            return c == 0 or c == 2 and slot > 0

        def known_below(t, bound):
            return isinstance(t, int) and t < bound

        def in_range(t):
            return not isinstance(t, int) or 0 <= t < NT

        @block.sync
        def _(sp):
            sp.dma_start(w_sb[:, :], W[:, :]).then_inc(params_here, 16)
            for k in range(2):
                sp.dma_start(a_sb[:, k:k + 1], a[k * F:(k + 1) * F, :]).then_inc(params_here, 16)
            sp.dma_start(ent[:, :, 0:F], entity.rearrange("(c p) f -> p c f", p=P)).then_inc(ent_here, 16)
            sp.dma_start(x_all, x.rearrange("(t p) f -> p t f", p=P)).then_inc(x_all_here, 16)

            def load_tile(t, slot, r):
                for c in range(NC):
                    q = NC // 2 * t + c // 2
                    if not known_below(t, 1) or c >= 2:
                        sp.wait_ge(mask_ready[c % 2], q)
                    sp.dma_start(adj_buf[:, c % 2, :],
                                 adj[bass.ds(t * P, P), c * CH:(c + 1) * CH]).then_inc(adj_here[c % 2], 16)

            periods(sp, load_tile, NT)

        @block.gpsimd
        def _(pool):
            pool.memset(ent[:, :, F:FA], 1.0).then_inc(ones_ready, 1)
            pool.memset(ident[:, :], 0.0).then_inc(ident_step, 1)
            pool.wait_ge(ident_step, 1)
            pool.affine_select(out=ident[:, :], in_=ident[:, :], compare_op=ALU.not_equal, fill=1.0,
                               base=0, pattern=[[-1, P]], channel_multiplier=1).then_inc(ident_step, 1)
            pool.memset(ones[:, :], 1.0).then_inc(ones_ready, 1)
            pool.wait_ge(ones_ready, 2)

            def finish(t, slot, r):
                if not known_below(t, RING):
                    pool.wait_ge(stored[slot], 16 * r)
                pool.wait_ge(neg_ready, t + 1)
                pool.tensor_tensor(out_tile[:, slot, :], y_tile[:, slot, :], neg_tile[:, slot, :],
                                   ALU.add).then_inc(out_step, 1)
                pool.wait_ge(exp_ready, t + 1)
                pool.tensor_tensor(exp_tile[:, slot, :], exp_tile[:, slot, :], ones[:, 0:F],
                                   ALU.subtract).then_inc(out_step, 1)
                pool.wait_ge(out_step, OUT_STEPS * t + 2)
                pool.tensor_tensor(out_tile[:, slot, :], out_tile[:, slot, :], exp_tile[:, slot, :],
                                   ALU.add).then_inc(out_step, 1)
                pool.wait_ge(out_step, OUT_STEPS * t + 3)
                pool.tensor_tensor(out_tile[:, slot, :], out_tile[:, slot, :], x_tile[:, slot, :],
                                   ALU.add).then_inc(out_step, 1)

            periods(pool, finish, NT)

        @block.scalar
        def _(act):
            for q in range(NS):
                act.wait_ge(entT_turned, q + 1)
                nc.scalar.activation(entT[:, q * BANK:(q + 1) * BANK],
                                     turned[0:F, q % 2, 0:BANK // P, :], ACT.Copy).then_inc(entT_copied, 1)
            act.wait_ge(ent_summed, 1)
            nc.scalar.activation(ent_sum[:, :], ent_sum_ps, ACT.Copy).then_inc(ent_sum_copied, 1)
            act.wait_ge(ln_step, 6)
            nc.scalar.activation(rstd, var[:, :], ACT.Sqrt).then_inc(std_ready, 1)

            def make_relu(t, slot, c):
                n = NC * t + c
                act.wait_ge(z_ready, n + 1)
                if not known_below(t, 1) or c >= 2:
                    act.wait_ge(shifted, n - 1)
                act.wait_ge(row_copied, t + 1)
                nc.scalar.activation(relu_buf[:, c % 2, :], logits[:, slot, c * CH:(c + 1) * CH], ACT.Relu,
                                     bias=row[:, slot, 0:1], scale=4.0).then_inc(relu_ready, 1)

            def make_mask(t, c):
                q = NC // 2 * t + c // 2
                act.wait_ge(adj_here[c % 2], 16 * (q + 1))
                if not known_below(t, 1) or c >= 2:
                    act.wait_ge(z_ready, NC * t + c - 1)
                nc.scalar.activation(mask_buf[:, c % 2, :], adj_buf[:, c % 2, :], ACT.Relu, bias=1.0,
                                     scale=-1.0).then_inc(mask_ready[c % 2], 1)

            def make_weights(t, b):
                act.wait_ge(block_turned, NB * t + b + 1)
                if not known_below(t, 1) or b >= 2:
                    act.wait_ge(block_summed, NB * t + b - 1)
                nc.scalar.activation(weights[:, b % 2, :, :], turned[:, b % 2, :, :],
                                     ACT.Exp).then_inc(weights_ready, 1)

            def make_h(t, slot, r):
                act.wait_ge(x_here[slot], 16 * (r + 1))
                if not known_below(t, RING):
                    act.wait_ge(y_ready, t - RING + 1)
                act.wait_ge(row_copied, t + 1)
                nc.scalar.activation(h_tile[:, slot, :], x_tile[:, slot, :], ACT.Relu,
                                     bias=row[:, slot, 2:3], scale=row[:, slot, 1:2]).then_inc(h_ready, 1)

            def make_neg(t, slot):
                act.wait_ge(y_ready, t + 1)
                if not known_below(t, RING):
                    act.wait_ge(out_step, OUT_STEPS * (t - RING + 1))
                nc.scalar.activation(neg_tile[:, slot, :], y_tile[:, slot, :], ACT.Relu,
                                     scale=-1.0).then_inc(neg_ready, 1)

            def make_exp(t, slot):
                act.wait_ge(neg_ready, t + 1)
                nc.scalar.activation(exp_tile[:, slot, :], neg_tile[:, slot, :], ACT.Exp,
                                     scale=-1.0).then_inc(exp_ready, 1)

            def load_x(t, slot):
                if not known_below(t, RING):
                    act.wait_ge(out_step, OUT_STEPS * (t - RING + 1))
                act.dma_start(x_tile[:, slot, :], x[bass.ds(t * P, P), :]).then_inc(x_here[slot], 16)

            def store_out(t, slot):
                act.wait_ge(out_step, OUT_STEPS * (t + 1))
                act.dma_start(out[bass.ds(t * P, P), :], out_tile[:, slot, :]).then_inc(stored[slot], 16)

            def period(t, slot, r):
                before, older = (slot - 1) % RING, (slot - 2) % RING
                for c in range(NC):
                    for half in range(BPC):
                        if c < 2 and in_range(t - 2):
                            make_weights(t - 2, (c + 2) * BPC + half)
                        if c >= 2 and in_range(t - 1):
                            make_weights(t - 1, (c - 2) * BPC + half)
                        if half == 0:
                            if c < NC - 1 and in_range(t - 1):
                                make_relu(t - 1, before, c + 1)
                            if c == NC - 1 and in_range(t):
                                make_relu(t, slot, 0)
                    if c == 0 and in_range(t - 5):
                        store_out(t - 5, older)
                    if c == 0 and in_range(t) and not mask_by_vector(slot, 2):
                        make_mask(t, 2)
                    if c == 1 and in_range(t):
                        make_mask(t, 3)
                    if c == 3 and in_range(t + 1):
                        make_mask(t + 1, 1)
                    if c == 2 and in_range(t - 4):
                        make_neg(t - 4, before)
                        make_exp(t - 4, before)
                    if c == 2 and in_range(t - 2):
                        make_h(t - 2, older, r if slot > 1 else r - 1)
                    if c == 3 and in_range(t - 1):
                        load_x(t - 1, before)

            make_mask(0, 1)
            periods(act, period, NT + 5)
            for slot in range(RING):
                act.wait_ge(stored[slot], 16 * len(range(slot, NT, RING)))

        @block.vector
        def _(dve):
            dve.wait_ge(params_here, 48)
            for k in range(2):
                dve.tensor_copy(a_wide[:, k, :], a_sb[:, k:k + 1].to_broadcast([F, P])).then_inc(wide_ready, 1)
            dve.wait_ge(wT_turned, 1)
            dve.tensor_copy(wT_sb[:, :], wT_ps).then_inc(wT_copied, 1)
            dve.wait_ge(u_done, 2)
            dve.tensor_copy(u2_wide[:, :], u2_ps).then_inc(u_copied, 1)
            dve.tensor_copy(u1_rows[:, 0, :], u1_ps).then_inc(u_copied, 1)

            def wide(col):
                return col.rearrange("p (t o) -> p t o", o=1).to_broadcast([P, NT, F])

            dve.wait_ge(x_all_here, 16)
            dve.tensor_reduce(mean[:, :], x_all, AX.X, ALU.add).then_inc(ln_step, 1)
            dve.wait_ge(ln_step, 1)
            dve.tensor_scalar(mean[:, :], mean[:, :], 1.0 / F, None, ALU.mult).then_inc(ln_step, 1)
            dve.wait_ge(ln_step, 2)
            dve.tensor_tensor(x_all, x_all, wide(mean[:, :]), ALU.subtract).then_inc(ln_step, 1)
            dve.wait_ge(ln_step, 3)
            dve.tensor_tensor(tmp_all, x_all, x_all, ALU.mult).then_inc(ln_step, 1)
            dve.wait_ge(ln_step, 4)
            dve.tensor_reduce(var[:, :], tmp_all, AX.X, ALU.add).then_inc(ln_step, 1)
            dve.wait_ge(ln_step, 5)
            dve.tensor_scalar(var[:, :], var[:, :], 1.0 / F, EPS, ALU.mult, ALU.add).then_inc(ln_step, 1)
            for q in range(NS):
                dve.wait_ge(s2_done, q + 1)
                dve.tensor_scalar(s2_rows[:, q * BANK:(q + 1) * BANK], sumsT[:, q % RING, :], UNIT, None,
                                  ALU.mult).then_inc(s2_copied, 1)
            dve.wait_ge(std_ready, 1)
            dve.reciprocal(rstd, rstd).then_inc(ln_step, 1)
            dve.wait_ge(ln_step, 7)
            dve.scalar_tensor_tensor(out=shift, in0=mean[:, :], scalar=-1.0, in1=rstd,
                                     op0=ALU.mult, op1=ALU.mult)
            dve.tensor_tensor(tmp_all, x_all, wide(rstd), ALU.mult).then_inc(ln_step, 1)
            dve.wait_ge(ln_step, 8)
            dve.wait_ge(u_copied, 2)
            dve.scalar_tensor_tensor(out=tmp_all, in0=tmp_all, scalar=0.0,
                                     in1=u1_rows[:, :, :].to_broadcast([P, NT, F]),
                                     op0=ALU.max, op1=ALU.mult).then_inc(ln_step, 1)
            dve.wait_ge(ln_step, 9)
            dve.tensor_reduce(s1x08, tmp_all, AX.X, ALU.add).then_inc(ln_step, 1)
            dve.wait_ge(ln_step, 10)
            dve.tensor_scalar(s1x08, s1x08, 1.0 - SLOPE, None, ALU.mult).then_inc(ln_step, 1)
            dve.wait_ge(ln_step, 11)

            def make_mask(t, c):
                q = NC // 2 * t + c // 2
                dve.wait_ge(adj_here[c % 2], 16 * (q + 1))
                if not known_below(t, 1) or c >= 2:
                    dve.wait_ge(z_ready, NC * t + c - 1)
                dve.tensor_scalar(mask_buf[:, c % 2, :], adj_buf[:, c % 2, :], 0.0, None,
                                  ALU.is_le).then_inc(mask_ready[c % 2], 1)

            def await_z(t, c):
                dve.wait_ge(mask_ready[c % 2], NC // 2 * t + c // 2 + 1)
                if not known_below(t, RING):
                    dve.wait_ge(block_turned, NB * (t - RING) + BPC * (c + 1))

            def make_z(t, slot, c):
                cols = slice(c * CH, (c + 1) * CH)
                dve.tensor_tensor_reduce(out=logits[:, slot, cols], in0=s2_rows[:, cols],
                                         in1=mask_buf[:, c % 2, :], scale=SLOPE / UNIT, scalar=LOWEST,
                                         op0=ALU.subtract, op1=ALU.max,
                                         accum_out=chunk_max[:, slot, c:c + 1]).then_inc(z_ready, 1)

            def row_copy(t, slot):
                if not known_below(t, RING):
                    dve.wait_ge(h_ready, t - RING + 1)
                dve.tensor_copy(row[:, slot, :], stats[:, bass.ds(t, 1), :].squeeze(1)).then_inc(row_copied, 1)

            def row_a(t, slot):
                dve.wait_ge(z_ready, NC * (t + 1))
                dve.tensor_reduce(row_max[:, slot:slot + 1], chunk_max[:, slot, :], AX.X,
                                  ALU.max).then_inc(row_step, 1)

            def row_b(t, slot):
                dve.wait_ge(row_copied, t + 1)
                dve.wait_ge(row_step, ROW_STEPS * t + 1)
                dve.tensor_scalar(row_lin[:, slot:slot + 1], row_max[:, slot:slot + 1], 4.0,
                                  row[:, slot, 0:1], ALU.mult, ALU.add).then_inc(row_step, 1)
                dve.tensor_scalar(row_bare[:, slot:slot + 1], row_max[:, slot:slot + 1], -0.5 * SLOPE / UNIT,
                                  HUGE, ALU.is_le, ALU.mult).then_inc(row_step, 1)

            def row_c(t, slot):
                dve.wait_ge(row_step, ROW_STEPS * t + 3)
                dve.scalar_tensor_tensor(out=row_w[:, slot:slot + 1], in0=row_lin[:, slot:slot + 1], scalar=0.0,
                                         in1=row_max[:, slot:slot + 1], op0=ALU.max,
                                         op1=ALU.add).then_inc(row_step, 1)

            def shift_logits(t, slot, c):
                dve.wait_ge(row_step, ROW_STEPS * (t + 1))
                dve.wait_ge(relu_ready, NC * t + c + 1)
                cols = slice(c * CH, (c + 1) * CH)
                dve.scalar_tensor_tensor(out=logits[:, slot, cols], in0=logits[:, slot, cols],
                                         scalar=row_w[:, slot:slot + 1], in1=relu_buf[:, c % 2, :],
                                         op0=ALU.subtract, op1=ALU.add).then_inc(shifted, 1)

            def copy_sums(t, slot):
                dve.wait_ge(block_summed, NB * (t + 1))
                if not known_below(t, 1):
                    dve.wait_ge(sums_turned, t)
                dve.tensor_copy(sumsT_sb[:, :], sumsT[0:FA, slot, 0:P]).then_inc(sumsT_copied, 1)

            def y_a(t, slot):
                dve.wait_ge(sums_turned, t + 1)
                if not known_below(t, 1):
                    dve.wait_ge(y_ready, t)
                dve.scalar_tensor_tensor(out=full_sums[:, :], in0=ent_sum[:, :], scalar=row_bare[:, slot:slot + 1],
                                         in1=sums[:, 0:FA], op0=ALU.mult, op1=ALU.add).then_inc(y_step, 1)

            def y_b(t):
                dve.wait_ge(y_step, Y_STEPS * t + 1)
                dve.reciprocal(inv_den[:, :], full_sums[:, F:FA]).then_inc(y_step, 1)

            def y_c(t, slot):
                dve.wait_ge(y_step, Y_STEPS * t + 2)
                dve.wait_ge(h_ready, t + 1)
                if not known_below(t, RING):
                    dve.wait_ge(out_step, OUT_STEPS * (t - RING + 1))
                dve.scalar_tensor_tensor(out=y_tile[:, slot, :], in0=full_sums[:, 0:F], scalar=inv_den[:, :],
                                         in1=h_tile[:, slot, :], op0=ALU.mult, op1=ALU.add).then_inc(y_ready, 1)

            def period(t, slot, r):
                before, older = (slot - 1) % RING, (slot - 2) % RING
                for c in range(NC):
                    if in_range(t):
                        if c == 3 and in_range(t + 1):
                            make_mask(t + 1, 0)
                        make_z(t, slot, c)
                    if c == 0 and in_range(t):
                        row_copy(t, slot)
                    if c == 0 and in_range(t - 1):
                        row_b(t - 1, before)
                    if c == 0 and in_range(t) and mask_by_vector(slot, 2):
                        make_mask(t, 2)
                    if c == 3 and in_range(t - 3):
                        y_b(t - 3)
                    if c < NC - 1 and in_range(t):
                        await_z(t, c + 1)
                    if c == NC - 1 and in_range(t + 1):
                        await_z(t + 1, 0)
                    if c == 0 and in_range(t - 1):
                        row_c(t - 1, before)
                    if in_range(t - 1):
                        shift_logits(t - 1, before, c)
                    if c == 2 and in_range(t - 3):
                        y_a(t - 3, slot)
                    if c == 3 and in_range(t - 3):
                        y_c(t - 3, slot)
                    if c == 3 and in_range(t - 2):
                        copy_sums(t - 2, older)
                if in_range(t):
                    row_a(t, slot)

            make_mask(0, 0)
            await_z(0, 0)
            dve.wait_ge(ent_sum_copied, 1)
            periods(dve, period, NT + 3)

        @block.tensor
        def _(pe):
            pe.wait_ge(params_here, 48)
            pe.wait_ge(ident_step, 2)
            pe.transpose(wT_ps, w_sb[:, :], ident[0:F, 0:F]).then_inc(wT_turned, 1)
            pe.wait_ge(ent_here, 16)
            pe.wait_ge(wide_ready, 2)
            pe.wait_ge(wT_copied, 1)
            pe.matmul(u2_ps, wT_sb[:, :], a_wide[:, 1, :], start=True, stop=True).then_inc(u_done, 1)
            pe.matmul(u1_ps, a_wide[:, 0, :], wT_sb[:, :], start=True, stop=True).then_inc(u_done, 1)

            def turn_entities(q):
                if q >= 2:
                    pe.wait_ge(entT_copied, q - 1)
                for k in range(BANK // P):
                    last = pe.transpose(turned[0:F, q % 2, k, :], ent[:, q * (BANK // P) + k, 0:F], ident[:, :])
                last.then_inc(entT_turned, 1)

            turn_entities(0)
            pe.wait_ge(u_copied, 1)
            for q in range(NS):
                if q + 1 < NS:
                    turn_entities(q + 1)
                pe.wait_ge(entT_copied, q + 1)
                if q >= RING:
                    pe.wait_ge(s2_copied, q - RING + 1)
                pe.matmul(sumsT[:, q % RING, :], u2_wide[:, :], entT[:, q * BANK:(q + 1) * BANK],
                          start=True, stop=True).then_inc(s2_done, 1)
            pe.wait_ge(u_copied, 2)
            pe.wait_ge(ones_ready, 2)
            for g in range(NJ):
                last = pe.matmul(ent_sum_ps, ones[:, :], ent[:, g, :], start=(g == 0), stop=(g == NJ - 1))
            last.then_inc(ent_summed, 1)
            pe.wait_ge(s2_copied, NS)

            def turn_block(t, slot, b):
                pe.wait_ge(shifted, NC * t + b // BPC + 1)
                if not known_below(t, 1) or b >= 2:
                    pe.wait_ge(weights_ready, NB * t + b - 1)
                for k in range(JB):
                    j = b * BLK + k * P
                    last = pe.transpose(turned[:, b % 2, k, :], logits[:, slot, j:j + P], ident[:, :])
                last.then_inc(block_turned, 1)

            def sum_block(t, slot, b):
                pe.wait_ge(weights_ready, NB * t + b + 1)
                if b == 0 and not known_below(t, RING):
                    pe.wait_ge(sumsT_copied, t - RING + 1)
                for k in range(JB):
                    g = b * JB + k
                    last = pe.matmul(sumsT[0:FA, slot, 0:P], ent[:, g, :], weights[:, b % 2, k, :],
                                     start=(g == 0), stop=(g == NJ - 1))
                last.then_inc(block_summed, 1)

            def turn_back(t):
                pe.wait_ge(sumsT_copied, t + 1)
                if not known_below(t, 1):
                    pe.wait_ge(y_step, Y_STEPS * t - 1)
                pe.transpose(sums[:, 0:FA], sumsT_sb[:, :], ident[0:FA, 0:FA]).then_inc(sums_turned, 1)

            def period(t, slot, r):
                for b in range(NB):
                    if b + 2 < NB and in_range(t):
                        turn_block(t, slot, b + 2)
                    if b + 2 >= NB and in_range(t + 1):
                        turn_block(t + 1, (slot + 1) % RING, b + 2 - NB)
                    if in_range(t):
                        sum_block(t, slot, b)
                    if b == 4 and in_range(t - 1):
                        turn_back(t - 1)

            turn_block(0, 0, 0)
            turn_block(0, 0, 1)
            periods(pe, period, NT + 1)


_INS = ['x', 'adj', 'L0_gnn_entity_embs', 'L0_gnn_W', 'L0_gnn_a']


def kernel(**inputs):
    import numpy as _np
    import concourse.bacc as _bacc
    from concourse import mybir as _mybir
    from concourse.bass_utils import run_bass_kernel_spmd as _run

    nc = _bacc.Bacc("TRN2", target_bir_lowering=False, num_devices=1)
    arrays, args = {}, []
    for name in _INS:
        v = _np.ascontiguousarray(inputs[name])
        arrays[f"in_{name}"] = v
        args.append(nc.dram_tensor(f"in_{name}", v.shape, _mybir.dt.from_np(v.dtype), kind="ExternalInput").ap())
    args.append(nc.dram_tensor("out_0", inputs['x'].shape, _mybir.dt.float32, kind="ExternalOutput").ap())
    graph_attention_kernel(nc, *args)
    r = _run(nc, [arrays], core_ids=[0])
    return r.results[0]["out_0"]
```

```python
import concourse.bass as bass
from concourse import mybir
from contextlib import ExitStack


def graph_attention_kernel(nc, x, adj, entity, W, a, out):
    F32, BF16, I32 = mybir.dt.float32, mybir.dt.bfloat16, mybir.dt.int32
    ALU = mybir.AluOpType
    ACT = mybir.ActivationFunctionType
    AX = mybir.AxisListType

    P = nc.NUM_PARTITIONS
    N, F = x.shape
    M = entity.shape[0]
    NT = N // P
    NJ = M // P
    CH = 2048
    NC = M // CH
    BLK = 1024
    NB = M // BLK
    JB = BLK // P
    BPC = CH // BLK
    FA = F + 1
    BANK = 512
    SLOPE = 0.2
    UNIT = 2.0 ** -60
    EPS = 1e-5
    LOWEST = -3.0e38
    HUGE = 2.0 ** 40
    RING = 3
    ROUNDS = NT // RING
    PARTS = 4
    JP, TP = NJ // PARTS, NT // PARTS
    PEELED = 3

    with ExitStack() as es:
        def sb(name, shape, dt=F32):
            return es.enter_context(nc.sbuf_tensor(name, shape, dt))

        def ps(name, shape):
            return es.enter_context(nc.psum_tensor(name, shape, F32))

        def sem(name):
            return es.enter_context(nc.semaphore(name))

        logits = sb("logits", [P, RING, M])
        adj_buf = sb("adj_buf", [P, 2, CH], I32)
        mask_buf = sb("mask_buf", [P, 2, CH], BF16)
        relu_buf = sb("relu_buf", [P, 2, CH])
        s2_rows = sb("s2_rows", [P, M])
        ent = sb("ent", [P, NJ, FA])
        weights = sb("weights", [P, 2, JB, P])
        ident = sb("ident", [P, P])
        w_sb = sb("w_sb", [F, F])
        wT_sb = sb("wT_sb", [F, F])
        a_sb = sb("a_sb", [F, 2])
        a_wide = sb("a_wide", [F, 2, P])
        u_rows = sb("u_rows", [P, 2, F])
        s2_cols = sb("s2_cols", [P, NJ])
        s2_parts = sb("s2_parts", [P, 3, NJ], BF16)
        ident_bf = sb("ident_bf", [P, P], BF16)
        mean = sb("mean", [P, NT])
        var = sb("var", [P, NT])
        stats = sb("stats", [P, NT, 3])
        row = sb("row", [P, RING, 3])
        chunk_max = sb("chunk_max", [P, RING, NC])
        row_max = sb("row_max", [P, RING])
        row_lin = sb("row_lin", [P, RING])
        row_w = sb("row_w", [P, RING])
        row_bare = sb("row_bare", [P, RING])
        sumsT_sb = sb("sumsT_sb", [FA, P])
        inv_den = sb("inv_den", [P, 1])
        full_sums = sb("full_sums", [P, FA])
        ent_sum = sb("ent_sum", [P, FA])
        ent_sumT = sb("ent_sumT", [FA, P])
        ones = sb("ones", [P, P])
        x_tile = sb("x_tile", [P, RING, F])
        h_tile = sb("h_tile", [P, RING, F])
        y_tile = sb("y_tile", [P, RING, F])
        neg_tile = sb("neg_tile", [P, RING, F])
        exp_tile = sb("exp_tile", [P, RING, F])
        out_tile = sb("out_tile", [P, RING, F])

        turned = ps("turned", [P, 2, JB, P])
        sumsT = ps("sumsT", [P, RING, BANK])
        sums = ps("sums", [P, BANK])

        ent_prod = logits[:, 1, 0:NJ * F].rearrange("p (t f) -> p t f", f=F)
        x_prod = logits[:, 1, NJ * F:NJ * F + NT * F].rearrange("p (t f) -> p t f", f=F)
        x_all = logits[:, 2, 0:NT * F].rearrange("p (t f) -> p t f", f=F)
        x_sq = logits[:, 2, NT * F:2 * NT * F].rearrange("p (t f) -> p t f", f=F)
        s1x08, rstd, shift = stats[:, :, 0], stats[:, :, 1], stats[:, :, 2]
        wT_ps, u_ps = sums[0:F, 0:F], sums[:, P:P + 2 * F].rearrange("p (k f) -> p k f", f=F)
        ent_sumT_ps, ent_sum_ps = sums[0:FA, 0:P], sums[:, 3 * P:3 * P + FA]

        params_here = sem("params_here")
        ent_here = [sem(f"ent_here{k}") for k in range(PARTS)]
        x_all_here = [sem(f"x_all_here{k}") for k in range(PARTS)]
        adj_here = [sem("adj_here0"), sem("adj_here1")]
        x_here = [sem(f"x_here{k}") for k in range(RING)]
        stored = [sem(f"stored{k}") for k in range(RING)]
        ident_step, ones_ready = sem("ident_step"), sem("ones_ready")
        wT_turned, wT_copied, wide_ready = sem("wT_turned"), sem("wT_copied"), sem("wide_ready")
        u_done, u_copied = sem("u_done"), sem("u_copied")
        s2_step, s2_done, s2_copied = sem("s2_step"), sem("s2_done"), sem("s2_copied")
        ent_sumT_done, ent_sumT_copied = sem("ent_sumT_done"), sem("ent_sumT_copied")
        mean_ready, x_centred, squared = sem("mean_ready"), sem("x_centred"), sem("squared")
        part_step, ln_step, std_ready = sem("part_step"), sem("ln_step"), sem("std_ready")
        mask_ready = [sem("mask_ready0"), sem("mask_ready1")]
        z_ready, relu_ready = sem("z_ready"), sem("relu_ready")
        row_copied, row_step, shifted = sem("row_copied"), sem("row_step"), sem("shifted")
        block_turned, weights_ready = sem("block_turned"), sem("weights_ready")
        block_summed, sumsT_copied = sem("block_summed"), sem("sumsT_copied")
        sums_turned, y_step = sem("sums_turned"), sem("y_step")
        ent_summed, ent_sum_copied = sem("ent_summed"), sem("ent_sum_copied")
        h_ready, y_ready, neg_ready = sem("h_ready"), sem("y_ready"), sem("neg_ready")
        exp_ready, joined, out_ready = sem("exp_ready"), sem("joined"), sem("out_ready")

        block = es.enter_context(nc.Block())

        NS = M // BANK
        GPB = BANK // P
        ROW_STEPS = 4
        PART_STEPS = 3
        Y_STEPS = 2

        def periods(engine, body, last):
            for t in range(PEELED * RING):
                body(t, t % RING, t // RING)
            with engine.Fori(PEELED, ROUNDS, 1) as r:
                for k in range(RING):
                    body(r * RING + k, k, r)
            for t in range(ROUNDS * RING, last):
                body(t, t % RING, t // RING)

        def mask_by_vector(slot, c):
            return c == 0 or c == 2 and slot == 0

        def known_below(t, bound):
            return isinstance(t, int) and t < bound

        def in_range(t):
            return not isinstance(t, int) or 0 <= t < NT

        @block.sync
        def _(sp):
            sp.dma_start(w_sb[:, :], W[:, :]).then_inc(params_here, 16)
            for k in range(2):
                sp.dma_start(a_sb[:, k:k + 1], a[k * F:(k + 1) * F, :]).then_inc(params_here, 16)
            for k in range(PARTS):
                sp.dma_start(x_all[:, k * TP:(k + 1) * TP, :],
                             x[k * TP * P:(k + 1) * TP * P, :].rearrange("(t p) f -> p t f", p=P)
                             ).then_inc(x_all_here[k], 16)
            for k in range(PARTS):
                sp.dma_start(ent[:, k * JP:(k + 1) * JP, 0:F],
                             entity[k * JP * P:(k + 1) * JP * P, :].rearrange("(c p) f -> p c f", p=P)
                             ).then_inc(ent_here[k], 16)

            def load_tile(t, slot, r):
                for c in range(NC):
                    q = NC // 2 * t + c // 2
                    if not known_below(t, 1) or c >= 2:
                        sp.wait_ge(mask_ready[c % 2], q)
                    sp.dma_start(adj_buf[:, c % 2, :],
                                 adj[bass.ds(t * P, P), c * CH:(c + 1) * CH]).then_inc(adj_here[c % 2], 16)

            periods(sp, load_tile, NT)

        @block.gpsimd
        def _(pool):
            pool.memset(ent[:, :, F:FA], 1.0).then_inc(ones_ready, 1)
            pool.memset(ident[:, :], 0.0).then_inc(ident_step, 1)
            pool.wait_ge(ident_step, 1)
            pool.affine_select(out=ident[:, :], in_=ident[:, :], compare_op=ALU.not_equal, fill=1.0,
                               base=0, pattern=[[-1, P]], channel_multiplier=1).then_inc(ident_step, 1)
            pool.memset(ones[:, :], 1.0).then_inc(ones_ready, 1)

        @block.scalar
        def _(act):
            def make_mask(t, c):
                q = NC // 2 * t + c // 2
                act.wait_ge(adj_here[c % 2], 16 * (q + 1))
                if not known_below(t, 1) or c >= 2:
                    act.wait_ge(z_ready, NC * t + c - 1)
                nc.scalar.activation(mask_buf[:, c % 2, :], adj_buf[:, c % 2, :], ACT.Relu, bias=1.0,
                                     scale=-1.0).then_inc(mask_ready[c % 2], 1)

            act.wait_ge(ident_step, 2)
            nc.scalar.activation(ident_bf[:, :], ident[:, :], ACT.Copy).then_inc(ident_step, 1)
            for k in range(PARTS):
                act.wait_ge(x_all_here[k], 16)
                for n in range(k * TP, (k + 1) * TP):
                    last = nc.scalar.activation(x_prod[:, n, :], x_all[:, n, :], ACT.Copy, scale=1.0 / F,
                                                accum_out=mean[:, n:n + 1])
                last.then_inc(mean_ready, 1)
            for k in range(PARTS):
                act.wait_ge(x_centred, k + 1)
                nc.scalar.activation(x_sq[:, k * TP:(k + 1) * TP, :], x_all[:, k * TP:(k + 1) * TP, :],
                                     ACT.Square).then_inc(squared, 1)
            act.wait_ge(ent_sumT_done, 1)
            nc.scalar.activation(ent_sumT[:, :], ent_sumT_ps, ACT.Copy).then_inc(ent_sumT_copied, 1)
            make_mask(0, 1)
            act.wait_ge(ent_summed, 1)
            nc.scalar.activation(ent_sum[:, :], ent_sum_ps, ACT.Copy).then_inc(ent_sum_copied, 1)
            for q in range(NS):
                act.wait_ge(s2_done, q + 1)
                nc.scalar.activation(s2_rows[:, q * BANK:(q + 1) * BANK], sumsT[:, q % RING, :], ACT.Copy,
                                     scale=UNIT).then_inc(s2_copied, 1)
                if q == NS // 2 - 1:
                    act.wait_ge(ln_step, 1)
                    nc.scalar.activation(rstd, var[:, :], ACT.Sqrt).then_inc(std_ready, 1)

            def make_relu(t, slot, c):
                n = NC * t + c
                act.wait_ge(z_ready, n + 1)
                if not known_below(t, 1) or c >= 2:
                    act.wait_ge(shifted, n - 1)
                act.wait_ge(row_copied, t + 1)
                nc.scalar.activation(relu_buf[:, c % 2, :], logits[:, slot, c * CH:(c + 1) * CH], ACT.Relu,
                                     bias=row[:, slot, 0:1], scale=4.0).then_inc(relu_ready, 1)

            def make_weights(t, b):
                act.wait_ge(block_turned, NB * t + b + 1)
                if not known_below(t, 1) or b >= 2:
                    act.wait_ge(block_summed, NB * t + b - 1)
                nc.scalar.activation(weights[:, b % 2, :, :], turned[:, b % 2, :, :],
                                     ACT.Exp).then_inc(weights_ready, 1)

            def make_h(t, slot, r):
                act.wait_ge(x_here[slot], 16 * (r + 1))
                if not known_below(t, RING):
                    act.wait_ge(y_ready, t - RING + 1)
                act.wait_ge(row_copied, t + 1)
                nc.scalar.activation(h_tile[:, slot, :], x_tile[:, slot, :], ACT.Relu,
                                     bias=row[:, slot, 2:3], scale=row[:, slot, 1:2]).then_inc(h_ready, 1)

            def make_neg(t, slot):
                act.wait_ge(y_ready, t + 1)
                if not known_below(t, RING):
                    act.wait_ge(exp_ready, t - RING + 1)
                nc.scalar.activation(neg_tile[:, slot, :], y_tile[:, slot, :], ACT.Relu,
                                     scale=-1.0).then_inc(neg_ready, 1)

            def make_exp(t, slot):
                act.wait_ge(neg_ready, t + 1)
                if not known_below(t, RING):
                    act.wait_ge(out_ready, t - RING + 1)
                nc.scalar.activation(exp_tile[:, slot, :], neg_tile[:, slot, :], ACT.Exp,
                                     scale=-1.0).then_inc(exp_ready, 1)

            def load_x(t, slot):
                if not known_below(t, RING):
                    act.wait_ge(joined, t - RING + 1)
                act.dma_start(x_tile[:, slot, :], x[bass.ds(t * P, P), :]).then_inc(x_here[slot], 16)

            def store_out(t, slot):
                act.wait_ge(out_ready, t + 1)
                act.dma_start(out[bass.ds(t * P, P), :], out_tile[:, slot, :]).then_inc(stored[slot], 16)

            def period(t, slot, r):
                before, older = (slot - 1) % RING, (slot - 2) % RING
                for c in range(NC):
                    for half in range(BPC):
                        if c < 2 and in_range(t - 2):
                            make_weights(t - 2, (c + 2) * BPC + half)
                        if c >= 2 and in_range(t - 1):
                            make_weights(t - 1, (c - 2) * BPC + half)
                        if half == 0:
                            if c < NC - 1 and in_range(t - 1):
                                make_relu(t - 1, before, c + 1)
                            if c == NC - 1 and in_range(t):
                                make_relu(t, slot, 0)
                    if c == 1 and in_range(t - 5):
                        store_out(t - 5, older)
                    if c == 0 and in_range(t) and not mask_by_vector(slot, 2):
                        make_mask(t, 2)
                    if c == 1 and in_range(t):
                        make_mask(t, 3)
                    if c == 3 and in_range(t + 1):
                        make_mask(t + 1, 1)
                    if c == 2 and in_range(t - 4):
                        make_neg(t - 4, before)
                        make_exp(t - 4, before)
                    if c == 2 and in_range(t - 2):
                        make_h(t - 2, older, r if slot > 1 else r - 1)
                    if c == 3 and in_range(t - 1):
                        load_x(t - 1, before)

            periods(act, period, NT + 5)
            for slot in range(RING):
                act.wait_ge(stored[slot], 16 * len(range(slot, NT, RING)))

        @block.vector
        def _(dve):
            dve.wait_ge(params_here, 48)
            for k in range(2):
                dve.tensor_copy(a_wide[:, k, :], a_sb[:, k:k + 1].to_broadcast([F, P])).then_inc(wide_ready, 1)
            dve.wait_ge(wT_turned, 1)
            dve.tensor_copy(wT_sb[:, :], wT_ps).then_inc(wT_copied, 1)
            dve.wait_ge(u_done, 2)
            dve.tensor_copy(u_rows[:, :, :], u_ps).then_inc(u_copied, 1)
            dve.wait_ge(u_copied, 1)

            def make_mask(t, c):
                q = NC // 2 * t + c // 2
                dve.wait_ge(adj_here[c % 2], 16 * (q + 1))
                if not known_below(t, 1) or c >= 2:
                    dve.wait_ge(z_ready, NC * t + c - 1)
                dve.tensor_scalar(mask_buf[:, c % 2, :], adj_buf[:, c % 2, :], 0.0, None,
                                  ALU.is_le).then_inc(mask_ready[c % 2], 1)

            for k in range(PARTS):
                part = slice(k * TP, (k + 1) * TP)
                done = 2 * k
                dve.wait_ge(mean_ready, k + 1)
                dve.tensor_tensor(x_all[:, part, :], x_all[:, part, :],
                                  mean[:, part].rearrange("p (t o) -> p t o", o=1).to_broadcast([P, TP, F]),
                                  ALU.subtract).then_inc(x_centred, 1)
                dve.wait_ge(x_centred, k + 1)
                dve.scalar_tensor_tensor(out=x_prod[:, part, :], in0=x_all[:, part, :], scalar=0.0,
                                         in1=u_rows[:, 0:1, :].to_broadcast([P, TP, F]),
                                         op0=ALU.max, op1=ALU.mult).then_inc(part_step, 1)
                dve.wait_ge(part_step, done + 1)
                dve.tensor_reduce(s1x08[:, part], x_prod[:, part, :], AX.X, ALU.add).then_inc(part_step, 1)
            for k in range(PARTS):
                part = slice(k * JP, (k + 1) * JP)
                dve.wait_ge(ent_here[k], 16)
                dve.tensor_tensor(ent_prod[:, part, :], ent[:, part, 0:F],
                                  u_rows[:, 1:2, :].to_broadcast([P, JP, F]), ALU.mult).then_inc(s2_step, 1)
                dve.wait_ge(s2_step, 2 * k + 1)
                dve.tensor_reduce(s2_cols[:, part], ent_prod[:, part, :], AX.X, ALU.add).then_inc(s2_step, 1)
            for k in range(3):
                dve.wait_ge(s2_step, 2 * PARTS + 2 * k)
                dve.tensor_copy(s2_parts[:, k, :], s2_cols[:, :]).then_inc(s2_step, 1)
                if k < 2:
                    dve.wait_ge(s2_step, 2 * PARTS + 2 * k + 1)
                    dve.tensor_tensor(s2_cols[:, :], s2_cols[:, :], s2_parts[:, k, :],
                                      ALU.subtract).then_inc(s2_step, 1)

            make_mask(0, 0)
            for k in range(PARTS):
                part = slice(k * TP, (k + 1) * TP)
                dve.wait_ge(squared, k + 1)
                dve.tensor_reduce(var[:, part], x_sq[:, part, :], AX.X, ALU.add).then_inc(part_step, 1)
            dve.wait_ge(part_step, PART_STEPS * PARTS)
            dve.tensor_scalar(var[:, :], var[:, :], 1.0 / F, EPS, ALU.mult, ALU.add).then_inc(ln_step, 1)

            def finish_stats():
                dve.wait_ge(std_ready, 1)
                dve.reciprocal(rstd, rstd).then_inc(ln_step, 1)
                dve.wait_ge(ln_step, 2)
                dve.scalar_tensor_tensor(out=shift, in0=mean[:, :], scalar=-1.0, in1=rstd,
                                         op0=ALU.mult, op1=ALU.mult).then_inc(ln_step, 1)
                dve.scalar_tensor_tensor(out=s1x08, in0=s1x08, scalar=1.0 - SLOPE, in1=rstd,
                                         op0=ALU.mult, op1=ALU.mult).then_inc(ln_step, 1)
                dve.wait_ge(ln_step, 4)

            def await_z(t, c):
                dve.wait_ge(mask_ready[c % 2], NC // 2 * t + c // 2 + 1)
                if known_below(t, 1):
                    dve.wait_ge(s2_copied, (c + 1) * CH // BANK)
                if not known_below(t, RING):
                    dve.wait_ge(block_turned, NB * (t - RING) + BPC * (c + 1))

            def make_z(t, slot, c):
                cols = slice(c * CH, (c + 1) * CH)
                dve.tensor_tensor_reduce(out=logits[:, slot, cols], in0=s2_rows[:, cols],
                                         in1=mask_buf[:, c % 2, :], scale=SLOPE / UNIT, scalar=LOWEST,
                                         op0=ALU.subtract, op1=ALU.max,
                                         accum_out=chunk_max[:, slot, c:c + 1]).then_inc(z_ready, 1)

            def row_copy(t, slot):
                if not known_below(t, RING):
                    dve.wait_ge(h_ready, t - RING + 1)
                dve.tensor_copy(row[:, slot, :], stats[:, bass.ds(t, 1), :].squeeze(1)).then_inc(row_copied, 1)

            def row_a(t, slot):
                dve.wait_ge(z_ready, NC * (t + 1))
                dve.tensor_reduce(row_max[:, slot:slot + 1], chunk_max[:, slot, :], AX.X,
                                  ALU.max).then_inc(row_step, 1)

            def row_b(t, slot):
                dve.wait_ge(row_copied, t + 1)
                dve.wait_ge(row_step, ROW_STEPS * t + 1)
                dve.tensor_scalar(row_lin[:, slot:slot + 1], row_max[:, slot:slot + 1], 4.0,
                                  row[:, slot, 0:1], ALU.mult, ALU.add).then_inc(row_step, 1)
                dve.tensor_scalar(row_bare[:, slot:slot + 1], row_max[:, slot:slot + 1], -0.5 * SLOPE / UNIT,
                                  HUGE, ALU.is_le, ALU.mult).then_inc(row_step, 1)

            def row_c(t, slot):
                dve.wait_ge(row_step, ROW_STEPS * t + 3)
                dve.scalar_tensor_tensor(out=row_w[:, slot:slot + 1], in0=row_lin[:, slot:slot + 1], scalar=0.0,
                                         in1=row_max[:, slot:slot + 1], op0=ALU.max,
                                         op1=ALU.add).then_inc(row_step, 1)

            def shift_logits(t, slot, c):
                dve.wait_ge(row_step, ROW_STEPS * (t + 1))
                dve.wait_ge(relu_ready, NC * t + c + 1)
                cols = slice(c * CH, (c + 1) * CH)
                dve.scalar_tensor_tensor(out=logits[:, slot, cols], in0=logits[:, slot, cols],
                                         scalar=row_w[:, slot:slot + 1], in1=relu_buf[:, c % 2, :],
                                         op0=ALU.subtract, op1=ALU.add).then_inc(shifted, 1)

            def copy_sums(t, slot):
                dve.wait_ge(block_summed, NB * (t + 1))
                if not known_below(t, 1):
                    dve.wait_ge(sums_turned, t)
                dve.tensor_copy(sumsT_sb[:, :], sumsT[0:FA, slot, 0:P]).then_inc(sumsT_copied, 1)

            def y_a(t, slot):
                dve.wait_ge(sums_turned, t + 1)
                if known_below(t, 1):
                    dve.wait_ge(ent_sum_copied, 1)
                else:
                    dve.wait_ge(y_ready, t)
                dve.scalar_tensor_tensor(out=full_sums[:, :], in0=ent_sum[:, :], scalar=row_bare[:, slot:slot + 1],
                                         in1=sums[:, 0:FA], op0=ALU.mult, op1=ALU.add).then_inc(y_step, 1)

            def y_b(t):
                dve.wait_ge(y_step, Y_STEPS * t + 1)
                dve.reciprocal(inv_den[:, :], full_sums[:, F:FA]).then_inc(y_step, 1)

            def y_c(t, slot):
                dve.wait_ge(y_step, Y_STEPS * t + 2)
                dve.wait_ge(h_ready, t + 1)
                if not known_below(t, RING):
                    dve.wait_ge(neg_ready, t - RING + 1)
                    dve.wait_ge(joined, t - RING + 1)
                dve.scalar_tensor_tensor(out=y_tile[:, slot, :], in0=full_sums[:, 0:F], scalar=inv_den[:, :],
                                         in1=h_tile[:, slot, :], op0=ALU.mult, op1=ALU.add).then_inc(y_ready, 1)

            def join(t, slot, r):
                dve.wait_ge(y_ready, t + 1)
                if not known_below(t, RING):
                    dve.wait_ge(stored[slot], 16 * r)
                dve.scalar_tensor_tensor(out=out_tile[:, slot, :], in0=y_tile[:, slot, :], scalar=0.0,
                                         in1=x_tile[:, slot, :], op0=ALU.max, op1=ALU.add).then_inc(joined, 1)

            def finish(t, slot):
                dve.wait_ge(joined, t + 1)
                dve.wait_ge(exp_ready, t + 1)
                dve.scalar_tensor_tensor(out=out_tile[:, slot, :], in0=exp_tile[:, slot, :], scalar=-1.0,
                                         in1=out_tile[:, slot, :], op0=ALU.add,
                                         op1=ALU.add).then_inc(out_ready, 1)

            def period(t, slot, r):
                before, older = (slot - 1) % RING, (slot - 2) % RING
                for c in range(NC):
                    if in_range(t):
                        if c == 3 and in_range(t + 1) and not known_below(t, 1):
                            make_mask(t + 1, 0)
                        make_z(t, slot, c)
                        if c == 3 and known_below(t, 1):
                            make_mask(t + 1, 0)
                        if c == 0 and known_below(t, 1):
                            finish_stats()
                    if c == 0 and in_range(t):
                        row_copy(t, slot)
                    if c == 1 and in_range(t - 5):
                        finish(t - 5, older)
                    if c == 1 and in_range(t - 4):
                        join(t - 4, before, r - 1 if slot > 0 else r - 2)
                    if c == 0 and in_range(t - 1):
                        row_b(t - 1, before)
                    if c == 0 and in_range(t) and mask_by_vector(slot, 2):
                        make_mask(t, 2)
                    if c == 3 and in_range(t - 3):
                        y_b(t - 3)
                    if c < NC - 1 and in_range(t):
                        await_z(t, c + 1)
                    if c == NC - 1 and in_range(t + 1):
                        await_z(t + 1, 0)
                    if c == 0 and in_range(t - 1):
                        row_c(t - 1, before)
                    if in_range(t - 1):
                        shift_logits(t - 1, before, c)
                    if c == 2 and in_range(t - 3):
                        y_a(t - 3, slot)
                    if c == 3 and in_range(t - 3):
                        y_c(t - 3, slot)
                    if c == 3 and in_range(t - 2):
                        copy_sums(t - 2, older)
                if in_range(t):
                    row_a(t, slot)

            await_z(0, 0)
            periods(dve, period, NT + 5)

        @block.tensor
        def _(pe):
            pe.wait_ge(params_here, 48)
            pe.wait_ge(ident_step, 2)
            pe.transpose(wT_ps, w_sb[:, :], ident[0:F, 0:F]).then_inc(wT_turned, 1)
            pe.wait_ge(wide_ready, 2)
            pe.wait_ge(wT_copied, 1)
            for k in range(2):
                pe.matmul(u_ps[:, k, :], a_wide[:, k, :], wT_sb[:, :], start=True, stop=True).then_inc(u_done, 1)

            pe.wait_ge(u_copied, 1)
            pe.wait_ge(ones_ready, 2)
            for g in range(NJ):
                if g % JP == 0:
                    pe.wait_ge(ent_here[g // JP], 16)
                last = pe.matmul(ent_sumT_ps, ent[:, g, :], ones[:, :], start=(g == 0), stop=(g == NJ - 1))
            last.then_inc(ent_sumT_done, 1)
            pe.wait_ge(ent_sumT_copied, 1)
            pe.transpose(ent_sum_ps, ent_sumT[:, :], ident[0:FA, 0:FA]).then_inc(ent_summed, 1)

            pe.wait_ge(ident_step, 3)
            pe.wait_ge(s2_step, 2 * PARTS + 5)
            for q in range(NS):
                if q >= RING:
                    pe.wait_ge(s2_copied, q - RING + 1)
                for n in range(GPB):
                    g = q * GPB + n
                    for k in range(3):
                        last = pe.matmul(sumsT[:, q % RING, n * P:(n + 1) * P],
                                         s2_parts[:, k, g:g + 1].to_broadcast([P, P]), ident_bf[:, :],
                                         start=(k == 0), stop=(k == 2))
                last.then_inc(s2_done, 1)

            pe.wait_ge(s2_copied, NS)

            def turn_block(t, slot, b):
                pe.wait_ge(shifted, NC * t + b // BPC + 1)
                if not known_below(t, 1) or b >= 2:
                    pe.wait_ge(weights_ready, NB * t + b - 1)
                for k in range(JB):
                    j = b * BLK + k * P
                    last = pe.transpose(turned[:, b % 2, k, :], logits[:, slot, j:j + P], ident[:, :])
                last.then_inc(block_turned, 1)

            def sum_block(t, slot, b):
                pe.wait_ge(weights_ready, NB * t + b + 1)
                if b == 0 and not known_below(t, RING):
                    pe.wait_ge(sumsT_copied, t - RING + 1)
                for k in range(JB):
                    g = b * JB + k
                    last = pe.matmul(sumsT[0:FA, slot, 0:P], ent[:, g, :], weights[:, b % 2, k, :],
                                     start=(g == 0), stop=(g == NJ - 1))
                last.then_inc(block_summed, 1)

            def turn_back(t):
                pe.wait_ge(sumsT_copied, t + 1)
                if not known_below(t, 1):
                    pe.wait_ge(y_step, Y_STEPS * t - 1)
                pe.transpose(sums[:, 0:FA], sumsT_sb[:, :], ident[0:FA, 0:FA]).then_inc(sums_turned, 1)

            def period(t, slot, r):
                for b in range(NB):
                    if b + 2 < NB and in_range(t):
                        turn_block(t, slot, b + 2)
                    if b + 2 >= NB and in_range(t + 1):
                        turn_block(t + 1, (slot + 1) % RING, b + 2 - NB)
                    if in_range(t):
                        sum_block(t, slot, b)
                    if b == 4 and in_range(t - 1):
                        turn_back(t - 1)

            turn_block(0, 0, 0)
            turn_block(0, 0, 1)
            periods(pe, period, NT + 1)


_INS = ['x', 'adj', 'L0_gnn_entity_embs', 'L0_gnn_W', 'L0_gnn_a']


def kernel(**inputs):
    import numpy as _np
    import concourse.bacc as _bacc
    from concourse import mybir as _mybir
    from concourse.bass_utils import run_bass_kernel_spmd as _run

    nc = _bacc.Bacc("TRN2", target_bir_lowering=False, num_devices=1)
    arrays, args = {}, []
    for name in _INS:
        v = _np.ascontiguousarray(inputs[name])
        arrays[f"in_{name}"] = v
        args.append(nc.dram_tensor(f"in_{name}", v.shape, _mybir.dt.from_np(v.dtype), kind="ExternalInput").ap())
    args.append(nc.dram_tensor("out_0", inputs['x'].shape, _mybir.dt.float32, kind="ExternalOutput").ap())
    graph_attention_kernel(nc, *args)
    r = _run(nc, [arrays], core_ids=[0])
    return r.results[0]["out_0"]
```
